# Optimizing a Trainium2 kernel written in Bass

```python
import numpy as np
import jax
import jax.numpy as jnp

def _softmax(x, axis=-1):
    return jax.nn.softmax(x, axis=axis)

def _gelu(x):
    return jax.nn.gelu(x, approximate=True)

def _silu(x):
    return jax.nn.silu(x)

def _sigmoid(x):
    return jax.nn.sigmoid(x)

def _layernorm(x, axis=-1, eps=1e-05):
    m = jnp.mean(x, axis=axis, keepdims=True)
    v = jnp.var(x, axis=axis, keepdims=True)
    return (x - m) / jnp.sqrt(v + eps)

def _scatter_add(tgt, idx, src, axis=0):
    return tgt.at[idx].add(src)

def _segment_sum(src, seg, n):
    return jax.ops.segment_sum(src, seg, n)
kernel_name = 'mk_xattn_seq_d1_seqx_r2_58c9fb'

def setup_inputs(seed: int=0):
    np.random.seed(seed)
    _w = jnp.asarray

    def _rec_inputs():
        import jax
        import jax.numpy as jnp
        _rk = jax.random.key(seed)
        x = -0.0003929 + 0.9999 * jax.random.normal(jax.random.fold_in(_rk, 1), (64, 512, 512), jnp.float32)
        _lenS = 512 - jax.random.randint(jax.random.fold_in(_rk, 7), (64,), 0, max(1, 512 // 4) + 1, jnp.int32)
        _lenS2 = 77 - jax.random.randint(jax.random.fold_in(_rk, 8), (64,), 0, max(1, 77 // 4) + 1, jnp.int32)
        _ctx_1024P = jax.random.normal(jax.random.fold_in(_rk, 11), (64, 16, 512), jnp.float32)
        _ctx_1024c = jax.random.dirichlet(jax.random.fold_in(_rk, 511), 0.3 * jnp.ones((16,), jnp.float32), (64, 77))
        _ctx_1024t = jnp.einsum('bsk,bkd->bsd', _ctx_1024c, _ctx_1024P)
        _ctx_1024t = _ctx_1024t * jax.lax.rsqrt(jnp.mean(jnp.square(_ctx_1024t)) + 1e-12) * 0.953939
        ctx_1024 = 2.81802e-05 + 1.00001 * (_ctx_1024t + 0.3 * jax.random.normal(jax.random.fold_in(_rk, 611), (64, 77, 512), jnp.float32))
        return (x, ctx_1024)
    x, ctx_1024 = _rec_inputs()

    def _L0_xattn_setup():
        import jax, jax.numpy as jnp
        import numpy as np
        B, SR, SF, D = (8, 1024, 1024, 512)
        key = jax.random.key(seed)
        k1, k2 = jax.random.split(key)
        H_real = jax.random.normal(k1, (B, SR, D), dtype=jnp.float32)
        H_fake = jax.random.normal(k2, (B, SF, D), dtype=jnp.float32)
        return {'H_real': H_real, 'H_fake': H_fake}
    _L0_xattn_all = _L0_xattn_setup()
    _L0_xattn_in = {k: v for k, v in _L0_xattn_all.items() if k in ()}
    del _L0_xattn_all
    return {'x': x, 'ctx_1024': ctx_1024}

def reference(x, ctx_1024):
    import jax
    import jax.numpy as jnp

    def _L0_xattn_ref(H_real, H_fake):
        import jax, jax.numpy as jnp
        import numpy as np
        B, SR, SF, D = (8, 1024, 1024, 512)
        scores = jnp.einsum('brd,bfd->brf', H_real, H_fake)
        weights = jax.nn.softmax(scores, axis=-1)
        context = jnp.einsum('brf,bfd->brd', weights, H_fake)
        return H_real + context
    x = _L0_xattn_ref(x, ctx_1024)
    return x

_drawn_inputs = setup_inputs


def setup_inputs(seed=0):
    import zlib

    import numpy as np

    out = dict(_drawn_inputs(seed))
    spreads = {}
    factors = {}
    for name, (base, spread) in spreads.items():
        noise = np.random.default_rng([zlib.crc32(name.encode()), seed]).standard_normal(out[name].shape)
        drawn = base * np.exp(spread * noise) if base else spread * noise
        out[name] = jnp.asarray(drawn.astype(out[name].dtype))
    for name, factor in factors.items():
        out[name] = (out[name] * factor).astype(out[name].dtype)
    return out
```

```python
from contextlib import ExitStack

import concourse.bass as bass
from concourse import mybir

F32 = mybir.dt.float32
F32R = mybir.dt.float32r
ALU = mybir.AluOpType
ACT = mybir.ActivationFunctionType
AX = mybir.AxisListType

P = 128
UNROLL = 6
AHEAD = 3
DMA = 16


class Batch:

    def __init__(self, i, offset):
        assert offset >= 0
        self.index = i * UNROLL + offset
        self.slot = offset % UNROLL
        self.parity = offset % 2
        self.round = i + offset // UNROLL
        self.offset = offset


def cross_attention(nc, xT, ctxT, outT):
    B, _, C, R = xT.shape
    K = ctxT.shape[3]
    T = R // P
    assert UNROLL % 2 == 0 and 2 < AHEAD and C * R * 4 <= 4 * 2048

    PEEL = 2 + (B - 2) % UNROLL
    ROUNDS = (B - PEEL) // UNROLL

    with ExitStack() as stack:
        def sbuf(name, shape, dtype=F32):
            return stack.enter_context(nc.sbuf_tensor(name, shape, dtype))

        def psum(name, shape):
            return stack.enter_context(nc.psum_tensor(name, shape, F32))

        def semaphore(name):
            return stack.enter_context(nc.semaphore(name))

        x_sb = [sbuf(f"x_sb{s}", [P, C, R]) for s in range(UNROLL)]
        ctxT_sb = [sbuf(f"ctxT_sb{s}", [P, C, K]) for s in range(UNROLL)]
        identity = sbuf("identity", [P, P])
        neg_max = [sbuf(f"neg_max{s}", [P, T]) for s in range(2)]
        exps = [sbuf(f"exps{s}", [P, T, K]) for s in range(2)]
        row_sum = [sbuf(f"row_sum{s}", [P, T]) for s in range(2)]
        inv_sum = [sbuf(f"inv_sum{s}", [P, T]) for s in range(2)]
        probs = [sbuf(f"probs{s}", [P, T, K]) for s in range(2)]
        pT_high = [sbuf(f"pT_high{s}", [K, R], F32R) for s in range(2)]
        pT_low = [sbuf(f"pT_low{s}", [K, R], F32R) for s in range(2)]
        ctx_high = [sbuf(f"ctx_high{s}", [K, C * P], F32R) for s in range(2)]
        ctx_low = [sbuf(f"ctx_low{s}", [K, C * P], F32R) for s in range(2)]

        scores = [psum(f"scores{s}", [P, 512]) for s in range(2)]
        pT_ps = psum("pT_ps", [P, 512])
        ctx_ps = psum("ctx_ps", [P, 512])
        context = [psum(f"context{c}", [P, R]) for c in range(C)]

        x_loaded = [semaphore(f"x_loaded{s}") for s in range(UNROLL)]
        ctx_loaded = [semaphore(f"ctx_loaded{s}") for s in range(UNROLL)]
        stored = [semaphore(f"stored{s}") for s in range(UNROLL)]
        identity_zeroed = semaphore("identity_zeroed")
        identity_ready = semaphore("identity_ready")
        scores_ready = semaphore("scores_ready")
        neg_max_ready = semaphore("neg_max_ready")
        exps_ready = semaphore("exps_ready")
        inv_sum_ready = semaphore("inv_sum_ready")
        probs_ready = semaphore("probs_ready")
        pT_ready = semaphore("pT_ready")
        ctx_turned = semaphore("ctx_turned")
        pT_high_ready = semaphore("pT_high_ready")
        pT_low_ready = semaphore("pT_low_ready")
        ctx_high_ready = semaphore("ctx_high_ready")
        ctx_low_ready = semaphore("ctx_low_ready")
        context_ready = semaphore("context_ready")
        chunk_added = semaphore("chunk_added")

        def tiles(bank):
            return bank[:, 0:T * K].rearrange("p (t k) -> p t k", t=T)

        def steps(engine, step):
            for t in range(PEEL):
                step(0, t)
            with engine.Fori(0, ROUNDS) as i:
                for u in range(UNROLL):
                    step(i, PEEL + u)
            for t in range(B, B + 2):
                step(0, t)

        block = stack.enter_context(nc.Block())

        @block.sync
        def _(sp):
            def load(b):
                sp.dma_start(ctxT_sb[b.slot][:], ctxT[b.index]).then_inc(ctx_loaded[b.slot], DMA)
                sp.dma_start(x_sb[b.slot][:], xT[b.index]).then_inc(x_loaded[b.slot], DMA)

            def step(i, t):
                if t >= 2:
                    b = Batch(i, t - 2)
                    sp.wait_ge(chunk_added, b.index * C + C)
                    sp.dma_start(outT[b.index], x_sb[b.slot][:]).then_inc(stored[b.slot], DMA)
                if t + AHEAD < B or (t < PEEL + UNROLL and t + AHEAD < B):
                    b = Batch(i, t + AHEAD)
                    if t + AHEAD >= UNROLL:
                        sp.wait_ge(stored[b.slot], b.round * DMA)
                    load(b)

            for t in range(AHEAD):
                load(Batch(0, t))
            for t in range(PEEL):
                step(0, t)
            with sp.Fori(0, ROUNDS - 1) as i:
                for u in range(UNROLL):
                    step(i, PEEL + u)
            for t in range(B - UNROLL, B + 2):
                step(0, t)
            for s in range(UNROLL):
                sp.wait_ge(stored[s], len(range(s, B, UNROLL)) * DMA)

        @block.gpsimd
        def _(pool):
            nc.gpsimd.memset(identity[:], 0.0).then_inc(identity_zeroed, 1)
            pool.wait_ge(identity_zeroed, 1)
            nc.gpsimd.affine_select(out=identity[:], in_=identity[:], compare_op=ALU.not_equal, fill=1.0,
                                    base=0, pattern=[[-1, P]], channel_multiplier=1).then_inc(identity_ready, 1)

            def step(i, t):
                if t < B:
                    b = Batch(i, t)
                    pool.wait_ge(inv_sum_ready, b.index + 1)
                    if t >= 2:
                        pool.wait_ge(pT_ready, b.index - 1)
                    nc.gpsimd.tensor_tensor(probs[b.parity][:], exps[b.parity][:],
                                            inv_sum[b.parity][:].unsqueeze(2).to_broadcast([P, T, K]),
                                            ALU.mult).then_inc(probs_ready, 1)

            steps(pool, step)

        @block.tensor
        def _(pe):
            pe.wait_ge(identity_ready, 1)

            def score(b):
                pe.wait_ge(ctx_loaded[b.slot], b.round * DMA + DMA)
                pe.wait_ge(x_loaded[b.slot], b.round * DMA + DMA)
                if b.offset >= 2:
                    pe.wait_ge(exps_ready, b.index - 1)
                for t in range(T):
                    for c in range(C):
                        last = nc.tensor.matmul(tiles(scores[b.parity])[:, t, :],
                                                x_sb[b.slot][:, c, t * P:(t + 1) * P],
                                                ctxT_sb[b.slot][:, c, :], start=(c == 0), stop=(c == C - 1))
                last.then_inc(scores_ready, 1)

            def turn(b):
                if b.offset >= 1:
                    pe.wait_ge(ctx_low_ready, b.index)
                for c in range(C):
                    last = nc.tensor.transpose(ctx_ps[0:K, c * P:(c + 1) * P], ctxT_sb[b.slot][:, c, :],
                                               identity[:])
                last.then_inc(ctx_turned, 1)
                pe.wait_ge(probs_ready, b.index + 1)
                if b.offset >= 1:
                    pe.wait_ge(pT_low_ready, b.index)
                for t in range(T):
                    last = nc.tensor.transpose(pT_ps[0:K, t * P:(t + 1) * P], probs[b.parity][:, t, :],
                                               identity[:])
                last.then_inc(pT_ready, 1)

            def attend(b):
                pe.wait_ge(pT_low_ready, b.index + 1)
                pe.wait_ge(ctx_low_ready, b.index + 1)
                s = b.parity
                for c in range(C):
                    if b.offset >= 1:
                        pe.wait_ge(chunk_added, b.index * C - C + c + 1)
                    chunk = slice(c * P, (c + 1) * P)
                    nc.tensor.matmul(context[c][:], ctx_high[s][:, chunk], pT_high[s][:], start=True, stop=False)
                    nc.tensor.matmul(context[c][:], ctx_high[s][:, chunk], pT_low[s][:], start=False, stop=False)
                    nc.tensor.matmul(context[c][:], ctx_low[s][:, chunk], pT_high[s][:], start=False,
                                     stop=True).then_inc(context_ready, 1)

            def step(i, t):
                if t < B:
                    score(Batch(i, t))
                if 1 <= t < B + 1:
                    turn(Batch(i, t - 1))
                if t >= 2:
                    attend(Batch(i, t - 2))

            steps(pe, step)

        @block.scalar
        def _(act):
            def step(i, t):
                if 1 <= t < B + 1:
                    b = Batch(i, t - 1)
                    s = b.parity
                    act.wait_ge(ctx_turned, b.index + 1)
                    if t >= 3:
                        act.wait_ge(context_ready, b.index * C - C)
                    nc.scalar.activation(ctx_high[s][:], ctx_ps[0:K, :], ACT.Copy).then_inc(ctx_high_ready, 1)
                    act.wait_ge(pT_ready, b.index + 1)
                    nc.scalar.activation(pT_high[s][:], pT_ps[0:K, :], ACT.Copy).then_inc(pT_high_ready, 1)
                if t < B:
                    b = Batch(i, t)
                    s = b.parity
                    act.wait_ge(neg_max_ready, b.index + 1)
                    if t >= 2:
                        act.wait_ge(probs_ready, b.index - 1)
                    for r in range(T):
                        last = nc.scalar.activation(exps[s][:, r, :], tiles(scores[s])[:, r, :], ACT.Exp,
                                                    bias=neg_max[s][:, r:r + 1],
                                                    accum_out=row_sum[s][:, r:r + 1])
                    last.then_inc(exps_ready, 1)

            steps(act, step)

        @block.vector
        def _(dve):
            def add(b, c):
                dve.wait_ge(context_ready, b.index * C + c + 1)
                x = x_sb[b.slot][:, c, :]
                nc.vector.tensor_tensor(x, context[c][:], x, ALU.add).then_inc(chunk_added, 1)

            def low(b, bank, high, low_part, high_ready, done):
                dve.wait_ge(high_ready, b.index + 1)
                nc.vector.tensor_tensor(low_part[b.parity][:], bank[0:K, :], high[b.parity][:].bitcast(F32),
                                        ALU.subtract).then_inc(done, 1)

            def step(i, t):
                if t < B:
                    b = Batch(i, t)
                    dve.wait_ge(scores_ready, b.index + 1)
                    if t >= 2:
                        dve.wait_ge(exps_ready, b.index - 1)
                    nc.vector.tensor_reduce(neg_max[b.parity][:], tiles(scores[b.parity]), AX.X, ALU.max,
                                            negate=True).then_inc(neg_max_ready, 1)
                if 1 <= t < B + 1:
                    b = Batch(i, t - 1)
                    if t >= 3:
                        dve.wait_ge(context_ready, b.index * C - C)
                    low(b, ctx_ps, ctx_high, ctx_low, ctx_high_ready, ctx_low_ready)
                    low(b, pT_ps, pT_high, pT_low, pT_high_ready, pT_low_ready)
                if t >= 2:
                    for c in range(C):
                        add(Batch(i, t - 2), c)
                if t < B:
                    b = Batch(i, t)
                    dve.wait_ge(exps_ready, b.index + 1)
                    if t >= 2:
                        dve.wait_ge(probs_ready, b.index - 1)
                    nc.vector.reciprocal(inv_sum[b.parity][:], row_sum[b.parity][:]).then_inc(inv_sum_ready, 1)

            steps(dve, step)


def kernel(x, ctx_1024):
    import numpy as np
    import concourse.bacc as bacc
    from concourse.bass_utils import run_bass_kernel_spmd

    B, R, D = x.shape
    K = ctx_1024.shape[1]
    C = D // P
    xT = np.ascontiguousarray(np.asarray(x).reshape(B, R, C, P).transpose(0, 3, 2, 1))
    ctxT = np.ascontiguousarray(np.asarray(ctx_1024).reshape(B, K, C, P).transpose(0, 3, 2, 1))

    nc = bacc.Bacc("TRN2", target_bir_lowering=False, num_devices=1)
    xT_dram = nc.dram_tensor("xT", xT.shape, F32, kind="ExternalInput").ap()
    ctxT_dram = nc.dram_tensor("ctxT", ctxT.shape, F32, kind="ExternalInput").ap()
    outT_dram = nc.dram_tensor("outT", xT.shape, F32, kind="ExternalOutput").ap()
    cross_attention(nc, xT_dram, ctxT_dram, outT_dram)
    result = run_bass_kernel_spmd(nc, [{"xT": xT, "ctxT": ctxT}], core_ids=[0])
    outT = result.results[0]["outT"]
    return np.ascontiguousarray(outT.transpose(0, 3, 2, 1)).reshape(B, R, D)
```

```python
from contextlib import ExitStack

import concourse.bass as bass
from concourse import mybir

F32 = mybir.dt.float32
F32R = mybir.dt.float32r
ALU = mybir.AluOpType
ACT = mybir.ActivationFunctionType
AX = mybir.AxisListType

P = 128
UNROLL = 10
Q = 32
AHEAD = UNROLL - 3
DMA = 16


class Batch:

    def __init__(self, i, offset):
        assert offset >= 0
        self.index = i * UNROLL + offset
        self.slot = offset % UNROLL
        self.parity = offset % 2
        self.round = i + offset // UNROLL
        self.offset = offset


def cross_attention(nc, xT, ctxT, outT):
    B, _, C, R = xT.shape
    K = ctxT.shape[3]
    T = R // P
    Z = K - 2 * Q
    assert 0 < Z and 2 * Z <= Q and R == C * P
    assert UNROLL % 2 == 0 and 2 < AHEAD and C * R * 4 <= 4 * 2048

    PEEL = 2 + (B - 2) % UNROLL
    ROUNDS = (B - PEEL) // UNROLL

    with ExitStack() as stack:
        def sbuf(name, shape, dtype=F32):
            return stack.enter_context(nc.sbuf_tensor(name, shape, dtype))

        def psum(name, shape):
            return stack.enter_context(nc.psum_tensor(name, shape, F32))

        def semaphore(name):
            return stack.enter_context(nc.semaphore(name))

        x_sb = [sbuf(f"x_sb{s}", [P, C, R]) for s in range(UNROLL)]
        ctxT_sb = [sbuf(f"ctxT_sb{s}", [P, C, K]) for s in range(UNROLL)]
        identity = sbuf("identity", [P, P])
        neg_max = [sbuf(f"neg_max{s}", [P, T]) for s in range(2)]
        exps = [sbuf(f"exps{s}", [P, T, K]) for s in range(2)]
        row_sum = [sbuf(f"row_sum{s}", [P, T]) for s in range(2)]
        inv_sum = [sbuf(f"inv_sum{s}", [P, T]) for s in range(2)]
        probs = [sbuf(f"probs{s}", [P, T, P]) for s in range(2)]
        ctx_cols = [sbuf(f"ctx_cols{s}", [P, C, P]) for s in range(2)]
        pT = [[sbuf(f"pT{s}_{n}", [P, R], F32R) for n in range(2)] for s in range(2)]
        ctx = [[sbuf(f"ctx{s}_{n}", [P, C * P], F32R) for n in range(2)] for s in range(2)]

        scores = [psum(f"scores{s}", [P, 512]) for s in range(2)]
        pT_ps = psum("pT_ps", [P, 512])
        ctx_ps = psum("ctx_ps", [P, 512])
        context = [psum(f"context{c}", [P, R]) for c in range(C)]

        x_loaded = [semaphore(f"x_loaded{s}") for s in range(UNROLL)]
        ctx_loaded = [semaphore(f"ctx_loaded{s}") for s in range(UNROLL)]
        stored = [semaphore(f"stored{s}") for s in range(UNROLL)]
        identity_zeroed = semaphore("identity_zeroed")
        identity_ready = semaphore("identity_ready")
        pads_zeroed = semaphore("pads_zeroed")
        scores_ready = semaphore("scores_ready")
        neg_max_ready = semaphore("neg_max_ready")
        exps_ready = semaphore("exps_ready")
        inv_sum_ready = semaphore("inv_sum_ready")
        probs_ready = semaphore("probs_ready")
        ctx_cols_ready = semaphore("ctx_cols_ready")
        probs_turned = semaphore("probs_turned")
        ctx_turned = semaphore("ctx_turned")
        ctx_high_ready = semaphore("ctx_high_ready")
        ctx_low_ready = semaphore("ctx_low_ready")
        probs_high_ready = semaphore("probs_high_ready")
        probs_low0_ready = semaphore("probs_low0_ready")
        probs_low_ready = semaphore("probs_low_ready")
        probs_stacked = semaphore("probs_stacked")
        context_ready = semaphore("context_ready")
        chunk_added = semaphore("chunk_added")

        def tiles(bank):
            return bank[:, 0:T * K].rearrange("p (t k) -> p t k", t=T)

        def steps(engine, step, looks_ahead=False):
            rounds = ROUNDS - 1 if looks_ahead else ROUNDS
            for t in range(PEEL):
                step(0, t)
            with engine.Fori(0, rounds) as i:
                for u in range(UNROLL):
                    step(i, PEEL + u)
            for t in range(PEEL + rounds * UNROLL, B + 2):
                step(0, t)

        block = stack.enter_context(nc.Block())

        @block.sync
        def _(sp):
            def load(b):
                sp.dma_start(ctxT_sb[b.slot][:], ctxT[b.index]).then_inc(ctx_loaded[b.slot], DMA)
                sp.dma_start(x_sb[b.slot][:], xT[b.index]).then_inc(x_loaded[b.slot], DMA)

            def step(i, t):
                if t >= 2:
                    b = Batch(i, t - 2)
                    sp.wait_ge(chunk_added, b.index * C + C)
                    sp.dma_start(outT[b.index], x_sb[b.slot][:]).then_inc(stored[b.slot], DMA)
                if UNROLL <= t + AHEAD < B:
                    b = Batch(i, t + AHEAD)
                    sp.wait_ge(stored[b.slot], b.round * DMA)
                    load(b)

            for t in range(UNROLL):
                load(Batch(0, t))
            steps(sp, step, looks_ahead=True)
            for s in range(UNROLL):
                sp.wait_ge(stored[s], len(range(s, B, UNROLL)) * DMA)

        @block.gpsimd
        def _(pool):
            nc.gpsimd.memset(identity[:], 0.0).then_inc(identity_zeroed, 1)
            pool.wait_ge(identity_zeroed, 1)
            nc.gpsimd.affine_select(out=identity[:], in_=identity[:], compare_op=ALU.not_equal, fill=1.0,
                                    base=0, pattern=[[-1, P]], channel_multiplier=1).then_inc(identity_ready, 1)

            def arrange_ctx(b):
                cols, source = ctx_cols[b.parity], ctxT_sb[b.slot]
                nc.gpsimd.tensor_copy(cols[:, :, 0:K], source[:])
                nc.gpsimd.tensor_copy(cols[:, :, K:K + Z], source[:, :, 2 * Q:K])
                nc.gpsimd.tensor_copy(cols[:, :, 3 * Q:P], source[:, :, 0:Q]).then_inc(ctx_cols_ready, 1)

            def normalise(b):
                scale = inv_sum[b.parity][:].unsqueeze(2)
                for cols, keys in ((slice(0, K), slice(0, K)), (slice(K, K + Z), slice(2 * Q, K)),
                                   (slice(3 * Q, P), slice(0, Q))):
                    source = exps[b.parity][:, :, keys]
                    last = nc.gpsimd.tensor_tensor(probs[b.parity][:, :, cols], source,
                                                   scale.to_broadcast(list(source.shape)), ALU.mult)
                last.then_inc(probs_ready, 1)

            def step(i, t):
                if t + 1 < B:
                    b = Batch(i, t + 1)
                    pool.wait_ge(ctx_loaded[b.slot], b.round * DMA + DMA)
                    if t >= 1:
                        pool.wait_ge(ctx_turned, b.index - 1)
                if t < B:
                    b = Batch(i, t)
                    if t >= 2:
                        pool.wait_ge(probs_turned, b.index - 1)
                    pool.wait_ge(inv_sum_ready, b.index + 1)
                    normalise(b)
                if t + 1 < B:
                    arrange_ctx(Batch(i, t + 1))

            pool.wait_ge(ctx_loaded[0], DMA)
            arrange_ctx(Batch(0, 0))
            steps(pool, step, looks_ahead=True)

        @block.tensor
        def _(pe):
            pe.wait_ge(identity_ready, 1)
            pe.wait_ge(pads_zeroed, 6)

            def score(b):
                pe.wait_ge(ctx_loaded[b.slot], b.round * DMA + DMA)
                pe.wait_ge(x_loaded[b.slot], b.round * DMA + DMA)
                if b.offset >= 2:
                    pe.wait_ge(exps_ready, b.index - 1)
                for t in range(T):
                    for c in range(C):
                        last = nc.tensor.matmul(tiles(scores[b.parity])[:, t, :],
                                                x_sb[b.slot][:, c, t * P:(t + 1) * P],
                                                ctxT_sb[b.slot][:, c, :], start=(c == 0), stop=(c == C - 1))
                last.then_inc(scores_ready, 1)

            def turn(b):
                pe.wait_ge(ctx_cols_ready, b.index + 1)
                if b.offset >= 1:
                    pe.wait_ge(ctx_low_ready, b.index)
                for c in range(C):
                    last = nc.tensor.transpose(ctx_ps[:, c * P:(c + 1) * P], ctx_cols[b.parity][:, c, :],
                                               identity[:])
                last.then_inc(ctx_turned, 1)
                pe.wait_ge(probs_ready, b.index + 1)
                if b.offset >= 1:
                    pe.wait_ge(probs_stacked, b.index)
                for t in range(T):
                    last = nc.tensor.transpose(pT_ps[:, t * P:(t + 1) * P], probs[b.parity][:, t, :],
                                               identity[:])
                last.then_inc(probs_turned, 1)

            def attend(b):
                pe.wait_ge(ctx_low_ready, b.index + 1)
                pe.wait_ge(probs_stacked, b.index + 1)
                for c in range(C):
                    if b.offset >= 1:
                        pe.wait_ge(chunk_added, b.index * C - C + c + 1)
                    for n in range(2):
                        last = nc.tensor.matmul(context[c][:], ctx[b.parity][n][:, c * P:(c + 1) * P],
                                                pT[b.parity][n][:], start=(n == 0), stop=(n == 1))
                    last.then_inc(context_ready, 1)

            def step(i, t):
                if t < B:
                    score(Batch(i, t))
                if 1 <= t < B + 1:
                    turn(Batch(i, t - 1))
                if t >= 2:
                    attend(Batch(i, t - 2))

            steps(pe, step)

        @block.scalar
        def _(act):
            def copy(out, in_):
                return nc.scalar.activation(out, in_, ACT.Copy)

            def split_high(b, t):
                stack0, stack1 = ctx[b.parity]
                act.wait_ge(ctx_turned, b.index + 1)
                if t >= 3:
                    act.wait_ge(context_ready, b.index * C - C)
                copy(stack0[:], ctx_ps[:])
                copy(stack1[3 * Q:P, :], ctx_ps[Q:2 * Q, :]).then_inc(ctx_high_ready, 1)
                act.wait_ge(probs_turned, b.index + 1)
                copy(pT[b.parity][1][:], pT_ps[:]).then_inc(probs_high_ready, 1)

            def complete(b):
                act.wait_ge(probs_low_ready, b.index + 1)
                copy(pT[b.parity][0][0:K, :], pT_ps[0:K, :]).then_inc(probs_stacked, 1)

            def step(i, t):
                if 1 <= t < B + 1:
                    split_high(Batch(i, t - 1), t)
                if t < B:
                    b = Batch(i, t)
                    s = b.parity
                    act.wait_ge(neg_max_ready, b.index + 1)
                    if t >= 2:
                        act.wait_ge(probs_ready, b.index - 1)
                    for r in range(T):
                        last = nc.scalar.activation(exps[s][:, r, :], tiles(scores[s])[:, r, :], ACT.Exp,
                                                    bias=neg_max[s][:, r:r + 1],
                                                    accum_out=row_sum[s][:, r:r + 1])
                    last.then_inc(exps_ready, 1)
                if 1 <= t < B + 1:
                    complete(Batch(i, t - 1))

            steps(act, step)

        @block.vector
        def _(dve):
            for s in range(2):
                for tile in (probs[s][:, :, K + Z:3 * Q], ctx_cols[s][:, :, K + Z:3 * Q], ctx[s][1][2 * Q:3 * Q, :].bitcast(F32)):
                    nc.vector.memset(tile, 0.0).then_inc(pads_zeroed, 1)

            def add(b, c):
                dve.wait_ge(context_ready, b.index * C + c + 1)
                x = x_sb[b.slot][:, c, :]
                nc.vector.tensor_tensor(x, context[c][:], x, ALU.add).then_inc(chunk_added, 1)

            def low(out, value, high):
                return nc.vector.tensor_tensor(out, value, high.bitcast(F32), ALU.subtract)

            def step(i, t):
                if t < B:
                    b = Batch(i, t)
                    dve.wait_ge(scores_ready, b.index + 1)
                    if t >= 2:
                        dve.wait_ge(exps_ready, b.index - 1)
                    nc.vector.tensor_reduce(neg_max[b.parity][:], tiles(scores[b.parity]), AX.X, ALU.max,
                                            negate=True).then_inc(neg_max_ready, 1)
                if 1 <= t < B + 1:
                    b = Batch(i, t - 1)
                    stack0, stack1 = ctx[b.parity]
                    if t >= 3:
                        dve.wait_ge(context_ready, b.index * C - C)
                    dve.wait_ge(ctx_high_ready, b.index + 1)
                    low(stack1[0:K, :], ctx_ps[0:K, :], stack0[0:K, :]).then_inc(ctx_low_ready, 1)
                if t >= 2:
                    add(Batch(i, t - 2), 0)
                if 1 <= t < B + 1:
                    b = Batch(i, t - 1)
                    stack0, stack1 = pT[b.parity]
                    dve.wait_ge(probs_high_ready, b.index + 1)
                    low(stack0[2 * Q:P, :], pT_ps[2 * Q:P, :], stack1[2 * Q:P, :]).then_inc(probs_low0_ready, 1)
                if t >= 2:
                    add(Batch(i, t - 2), 1)
                if 1 <= t < B + 1:
                    dve.wait_ge(probs_low0_ready, b.index + 1)
                    low(stack1[3 * Q:P, :], pT_ps[Q:2 * Q, :], stack1[Q:2 * Q, :]).then_inc(probs_low_ready, 1)
                if t < B:
                    b = Batch(i, t)
                    dve.wait_ge(exps_ready, b.index + 1)
                    if t >= 2:
                        dve.wait_ge(probs_ready, b.index - 1)
                    nc.vector.reciprocal(inv_sum[b.parity][:], row_sum[b.parity][:]).then_inc(inv_sum_ready, 1)
                if t >= 2:
                    for c in range(2, C):
                        add(Batch(i, t - 2), c)

            steps(dve, step)


def kernel(x, ctx_1024):
    import numpy as np
    import concourse.bacc as bacc
    from concourse.bass_utils import run_bass_kernel_spmd

    B, R, D = x.shape
    K = ctx_1024.shape[1]
    C = D // P
    xT = np.ascontiguousarray(np.asarray(x).reshape(B, R, C, P).transpose(0, 3, 2, 1))
    ctxT = np.ascontiguousarray(np.asarray(ctx_1024).reshape(B, K, C, P).transpose(0, 3, 2, 1))

    nc = bacc.Bacc("TRN2", target_bir_lowering=False, num_devices=1)
    xT_dram = nc.dram_tensor("xT", xT.shape, F32, kind="ExternalInput").ap()
    ctxT_dram = nc.dram_tensor("ctxT", ctxT.shape, F32, kind="ExternalInput").ap()
    outT_dram = nc.dram_tensor("outT", xT.shape, F32, kind="ExternalOutput").ap()
    cross_attention(nc, xT_dram, ctxT_dram, outT_dram)
    result = run_bass_kernel_spmd(nc, [{"xT": xT, "ctxT": ctxT}], core_ids=[0])
    outT = result.results[0]["outT"]
    return np.ascontiguousarray(outT.transpose(0, 3, 2, 1)).reshape(B, R, D)
```

```python
from contextlib import ExitStack

import concourse.bass as bass
from concourse import mybir

F32 = mybir.dt.float32
F32R = mybir.dt.float32r
ALU = mybir.AluOpType
ACT = mybir.ActivationFunctionType
AX = mybir.AxisListType

P = 128
UNROLL = 10
Q = 32
AHEAD = UNROLL - 3
DMA = 16


class Batch:

    def __init__(self, i, offset):
        assert offset >= 0
        self.index = i * UNROLL + offset
        self.slot = offset % UNROLL
        self.parity = offset % 2
        self.round = i + offset // UNROLL
        self.offset = offset


def cross_attention(nc, xT, ctxT, outT):
    B, _, T, C, _ = xT.shape
    K = ctxT.shape[3]
    R = T * P
    Z = K - 2 * Q
    assert 0 < Z and K + Z <= 3 * Q and R == C * P == 512
    assert UNROLL % 2 == 0 and 2 < AHEAD

    PEEL = (B - 1) % UNROLL
    ROUNDS = (B - 1) // UNROLL
    assert PEEL >= 3 and ROUNDS >= 2

    with ExitStack() as stack:
        def sbuf(name, shape, dtype=F32):
            return stack.enter_context(nc.sbuf_tensor(name, shape, dtype))

        def psum(name, shape):
            return stack.enter_context(nc.psum_tensor(name, shape, F32))

        def semaphore(name):
            return stack.enter_context(nc.semaphore(name))

        x_sb = [sbuf(f"x_sb{s}", [P, T, C, P]) for s in range(UNROLL)]
        ctxT_sb = [sbuf(f"ctxT_sb{s}", [P, C, K]) for s in range(UNROLL)]
        identity = sbuf("identity", [P, P])
        neg_max = [sbuf(f"neg_max{s}", [P, T]) for s in range(2)]
        exps = [sbuf(f"exps{s}", [P, T, K]) for s in range(2)]
        row_sum = [sbuf(f"row_sum{s}", [P, T]) for s in range(2)]
        inv_sum = [sbuf(f"inv_sum{s}", [P, T]) for s in range(2)]
        probs = [sbuf(f"probs{s}", [P, T, P]) for s in range(2)]
        ctx_cols = [sbuf(f"ctx_cols{s}", [P, C, P]) for s in range(2)]
        pT = [[sbuf(f"pT{s}_{n}", [P, R], F32R) for n in range(2)] for s in range(2)]
        ctx = [[sbuf(f"ctx{s}_{n}", [P, C * P], F32R) for n in range(2)] for s in range(2)]

        scores = [psum(f"scores{s}", [P, 512]) for s in range(2)]
        pT_ps = psum("pT_ps", [P, 512])
        ctx_ps = psum("ctx_ps", [P, 512])
        context = [psum(f"context{c}", [P, R]) for c in range(C)]

        x_loaded = [semaphore(f"x_loaded{s}") for s in range(UNROLL)]
        ctx_loaded = [semaphore(f"ctx_loaded{s}") for s in range(UNROLL)]
        first_loaded = [None] + [semaphore(f"first_loaded{t}") for t in range(1, T)]
        stored = [semaphore(f"stored{s}") for s in range(UNROLL)]
        identity_zeroed = semaphore("identity_zeroed")
        identity_ready = semaphore("identity_ready")
        pads_zeroed = semaphore("pads_zeroed")
        scores_ready = semaphore("scores_ready")
        neg_max_ready = semaphore("neg_max_ready")
        exps_ready = semaphore("exps_ready")
        inv_sum_ready = semaphore("inv_sum_ready")
        probs_ready = semaphore("probs_ready")
        ctx_cols_ready = semaphore("ctx_cols_ready")
        probs_turned = semaphore("probs_turned")
        ctx_turned = semaphore("ctx_turned")
        ctx_high_ready = semaphore("ctx_high_ready")
        ctx_low_ready = semaphore("ctx_low_ready")
        probs_high_ready = semaphore("probs_high_ready")
        probs_low0_ready = semaphore("probs_low0_ready")
        probs_low_ready = semaphore("probs_low_ready")
        probs_stacked = semaphore("probs_stacked")
        context_ready = semaphore("context_ready")
        chunk_added = semaphore("chunk_added")

        def tiles(bank):
            return bank[:, 0:T * K].rearrange("p (t k) -> p t k", t=T)

        def steps(engine, step, end, rounds=ROUNDS):
            for t in range(PEEL):
                step(0, t)
            with nc.Fori(0, rounds, engines=bass.OrderedEngineSet([engine.engine]), hint_back_edge=True) as i:
                for u in range(UNROLL):
                    step(i, PEEL + u)
            for t in range(PEEL + rounds * UNROLL, end):
                step(0, t)

        block = stack.enter_context(nc.Block())

        @block.sync
        def _(sp):
            def load(b):
                sp.dma_start(ctxT_sb[b.slot][:], ctxT[b.index]).then_inc(ctx_loaded[b.slot], DMA)
                if b.offset > 0:
                    sp.dma_start(x_sb[b.slot][:], xT[b.index]).then_inc(x_loaded[b.slot], DMA)
                    return
                for t in range(T):
                    sp.dma_start(x_sb[0][:, t], xT[0, :, t]).then_inc(first_loaded[t] if t else x_loaded[0], DMA)

            def store_by_chunk(b):
                for c in range(C):
                    sp.wait_ge(chunk_added, b.index * C + c + 1)
                    sp.dma_start(outT[b.index, :, :, c], x_sb[b.slot][:, :, c]).then_inc(stored[b.slot], DMA)

            def step(i, t):
                if t >= B:
                    store_by_chunk(Batch(i, t - 2))
                elif t >= 2:
                    b = Batch(i, t - 2)
                    sp.wait_ge(chunk_added, b.index * C + C)
                    sp.dma_start(outT[b.index], x_sb[b.slot][:]).then_inc(stored[b.slot], DMA)
                if UNROLL <= t + AHEAD < B:
                    b = Batch(i, t + AHEAD)
                    sp.wait_ge(stored[b.slot], b.round * DMA)
                    load(b)

            for t in range(UNROLL):
                load(Batch(0, t))
            steps(sp, step, rounds=ROUNDS - 1, end=B + 2)
            for s in range(UNROLL):
                by_chunk = s in ((B - 2) % UNROLL, (B - 1) % UNROLL)
                stores = len(range(s, B, UNROLL)) + (C - 1 if by_chunk else 0)
                sp.wait_ge(stored[s], stores * DMA)

        @block.gpsimd
        def _(pool):
            nc.gpsimd.memset(identity[:], 0.0).then_inc(identity_zeroed, 1)
            pool.wait_ge(identity_zeroed, 1)
            nc.gpsimd.affine_select(out=identity[:], in_=identity[:], compare_op=ALU.not_equal, fill=1.0,
                                    base=0, pattern=[[-1, P]], channel_multiplier=1).then_inc(identity_ready, 1)

            def arrange_ctx(b):
                cols, source = ctx_cols[b.parity], ctxT_sb[b.slot]
                nc.gpsimd.tensor_copy(cols[:, :, 0:K], source[:])
                nc.gpsimd.tensor_copy(cols[:, :, K:K + Z], source[:, :, 2 * Q:K])
                nc.gpsimd.tensor_copy(cols[:, :, 3 * Q:P], source[:, :, 0:Q]).then_inc(ctx_cols_ready, 1)

            def normalise(b):
                if b.offset >= 2:
                    pool.wait_ge(probs_turned, b.index - 1)
                pool.wait_ge(inv_sum_ready, b.index + 1)
                scale = inv_sum[b.parity][:].unsqueeze(2)
                for cols, keys in ((slice(0, K), slice(0, K)), (slice(K, K + Z), slice(2 * Q, K)),
                                   (slice(3 * Q, P), slice(0, Q))):
                    source = exps[b.parity][:, :, keys]
                    last = nc.gpsimd.tensor_tensor(probs[b.parity][:, :, cols], source,
                                                   scale.to_broadcast(list(source.shape)), ALU.mult)
                last.then_inc(probs_ready, 1)

            def step(i, t):
                b = Batch(i, t + 1)
                pool.wait_ge(ctx_loaded[b.slot], b.round * DMA + DMA)
                if t >= 1:
                    pool.wait_ge(ctx_turned, b.index - 1)
                normalise(Batch(i, t))
                arrange_ctx(b)

            pool.wait_ge(ctx_loaded[0], DMA)
            arrange_ctx(Batch(0, 0))
            steps(pool, step, end=B - 1)
            normalise(Batch(0, B - 1))

        @block.tensor
        def _(pe):
            pe.wait_ge(identity_ready, 1)
            pe.wait_ge(pads_zeroed, 6)

            def score(b):
                pe.wait_ge(ctx_loaded[b.slot], b.round * DMA + DMA)
                pe.wait_ge(x_loaded[b.slot], b.round * DMA + DMA)
                if b.offset >= 2:
                    pe.wait_ge(exps_ready, b.index - 1)
                for t in range(T):
                    if b.offset == 0 and t > 0:
                        pe.wait_ge(first_loaded[t], DMA)
                    for c in range(C):
                        last = nc.tensor.matmul(tiles(scores[b.parity])[:, t, :], x_sb[b.slot][:, t, c, :],
                                                ctxT_sb[b.slot][:, c, :], start=(c == 0), stop=(c == C - 1))
                last.then_inc(scores_ready, 1)

            def turn_ctx(b):
                pe.wait_ge(ctx_cols_ready, b.index + 1)
                if b.offset >= 1:
                    pe.wait_ge(ctx_low_ready, b.index)
                for c in range(C):
                    last = nc.tensor.transpose(ctx_ps[:, c * P:(c + 1) * P], ctx_cols[b.parity][:, c, :],
                                               identity[:])
                last.then_inc(ctx_turned, 1)

            def turn_probs(b):
                pe.wait_ge(probs_ready, b.index + 1)
                if b.offset >= 1:
                    pe.wait_ge(probs_stacked, b.index)
                for t in range(T):
                    last = nc.tensor.transpose(pT_ps[:, t * P:(t + 1) * P], probs[b.parity][:, t, :],
                                               identity[:])
                last.then_inc(probs_turned, 1)

            def attend(b):
                pe.wait_ge(ctx_low_ready, b.index + 1)
                pe.wait_ge(probs_stacked, b.index + 1)
                for c in range(C):
                    if b.offset >= 1:
                        pe.wait_ge(chunk_added, b.index * C - C + c + 1)
                    for n in range(2):
                        last = nc.tensor.matmul(context[c][:], ctx[b.parity][n][:, c * P:(c + 1) * P],
                                                pT[b.parity][n][:], start=(n == 0), stop=(n == 1))
                    last.then_inc(context_ready, 1)

            def step(i, t):
                if t >= 1:
                    turn_ctx(Batch(i, t - 1))
                score(Batch(i, t))
                if t >= 1:
                    turn_probs(Batch(i, t - 1))
                if t >= 2:
                    attend(Batch(i, t - 2))

            steps(pe, step, end=B)
            turn_ctx(Batch(0, B - 1))
            attend(Batch(0, B - 2))
            turn_probs(Batch(0, B - 1))
            attend(Batch(0, B - 1))

        @block.scalar
        def _(act):
            def copy(out, in_):
                return nc.scalar.activation(out, in_, ACT.Copy)

            def high_ctx(b):
                stack0, stack1 = ctx[b.parity]
                act.wait_ge(ctx_turned, b.index + 1)
                if b.offset >= 2:
                    act.wait_ge(context_ready, b.index * C - C)
                copy(stack0[:], ctx_ps[:])
                copy(stack1[3 * Q:P, :], ctx_ps[Q:2 * Q, :]).then_inc(ctx_high_ready, 1)

            def high_probs(b):
                act.wait_ge(probs_turned, b.index + 1)
                copy(pT[b.parity][1][:], pT_ps[:]).then_inc(probs_high_ready, 1)

            def complete_probs(b):
                act.wait_ge(probs_low_ready, b.index + 1)
                copy(pT[b.parity][0][0:K, :], pT_ps[0:K, :]).then_inc(probs_stacked, 1)

            def exponentiate(b):
                act.wait_ge(neg_max_ready, b.index + 1)
                if b.offset >= 2:
                    act.wait_ge(probs_ready, b.index - 1)
                s = b.parity
                for r in range(T):
                    last = nc.scalar.activation(exps[s][:, r, :], tiles(scores[s])[:, r, :], ACT.Exp,
                                                bias=neg_max[s][:, r:r + 1], accum_out=row_sum[s][:, r:r + 1])
                last.then_inc(exps_ready, 1)

            def step(i, t):
                if t >= 1:
                    high_ctx(Batch(i, t - 1))
                    high_probs(Batch(i, t - 1))
                exponentiate(Batch(i, t))
                if t >= 1:
                    complete_probs(Batch(i, t - 1))

            steps(act, step, end=B)
            high_ctx(Batch(0, B - 1))
            high_probs(Batch(0, B - 1))
            complete_probs(Batch(0, B - 1))

        @block.vector
        def _(dve):
            for s in range(2):
                for tile in (probs[s][:, :, K + Z:3 * Q], ctx_cols[s][:, :, K + Z:3 * Q],
                             ctx[s][1][2 * Q:3 * Q, :].bitcast(F32)):
                    nc.vector.memset(tile, 0.0).then_inc(pads_zeroed, 1)

            def add(b, c):
                dve.wait_ge(context_ready, b.index * C + c + 1)
                x = x_sb[b.slot][:, :, c, :]
                nc.vector.tensor_tensor(x, context[c][:].rearrange("p (t r) -> p t r", t=T), x,
                                        ALU.add).then_inc(chunk_added, 1)

            def low(out, value, high):
                return nc.vector.tensor_tensor(out, value, high.bitcast(F32), ALU.subtract)

            def low_ctx(b):
                stack0, stack1 = ctx[b.parity]
                if b.offset >= 2:
                    dve.wait_ge(context_ready, b.index * C - C)
                dve.wait_ge(ctx_high_ready, b.index + 1)
                low(stack1[0:K, :], ctx_ps[0:K, :], stack0[0:K, :]).then_inc(ctx_low_ready, 1)

            def low_probs0(b):
                stack0, stack1 = pT[b.parity]
                dve.wait_ge(probs_high_ready, b.index + 1)
                low(stack0[2 * Q:P, :], pT_ps[2 * Q:P, :], stack1[2 * Q:P, :]).then_inc(probs_low0_ready, 1)

            def low_probs1(b):
                stack1 = pT[b.parity][1]
                dve.wait_ge(probs_low0_ready, b.index + 1)
                low(stack1[3 * Q:P, :], pT_ps[Q:2 * Q, :], stack1[Q:2 * Q, :]).then_inc(probs_low_ready, 1)

            def find_max(b):
                dve.wait_ge(scores_ready, b.index + 1)
                if b.offset >= 2:
                    dve.wait_ge(exps_ready, b.index - 1)
                nc.vector.tensor_reduce(neg_max[b.parity][:], tiles(scores[b.parity]), AX.X, ALU.max,
                                        negate=True).then_inc(neg_max_ready, 1)

            def invert_sum(b):
                dve.wait_ge(exps_ready, b.index + 1)
                if b.offset >= 2:
                    dve.wait_ge(probs_ready, b.index - 1)
                nc.vector.reciprocal(inv_sum[b.parity][:], row_sum[b.parity][:]).then_inc(inv_sum_ready, 1)

            def step(i, t):
                if t >= 1:
                    low_ctx(Batch(i, t - 1))
                find_max(Batch(i, t))
                if t >= 2:
                    add(Batch(i, t - 2), 0)
                if t >= 1:
                    low_probs0(Batch(i, t - 1))
                if t >= 2:
                    add(Batch(i, t - 2), 1)
                if t >= 1:
                    low_probs1(Batch(i, t - 1))
                invert_sum(Batch(i, t))
                if t >= 2:
                    for c in range(2, C):
                        add(Batch(i, t - 2), c)

            steps(dve, step, end=B - 1)
            low_ctx(Batch(0, B - 2))
            find_max(Batch(0, B - 1))
            low_probs0(Batch(0, B - 2))
            low_probs1(Batch(0, B - 2))
            invert_sum(Batch(0, B - 1))
            for c in range(C):
                add(Batch(0, B - 3), c)
            low_ctx(Batch(0, B - 1))
            for c in range(2):
                add(Batch(0, B - 2), c)
            low_probs0(Batch(0, B - 1))
            low_probs1(Batch(0, B - 1))
            for c in range(2, C):
                add(Batch(0, B - 2), c)
            for c in range(C):
                add(Batch(0, B - 1), c)


def kernel(x, ctx_1024):
    import numpy as np
    import concourse.bacc as bacc
    from concourse.bass_utils import run_bass_kernel_spmd

    B, R, D = x.shape
    K = ctx_1024.shape[1]
    C = D // P
    T = R // P
    xT = np.ascontiguousarray(np.asarray(x).reshape(B, T, P, C, P).transpose(0, 4, 1, 3, 2))
    ctxT = np.ascontiguousarray(np.asarray(ctx_1024).reshape(B, K, C, P).transpose(0, 3, 2, 1))

    nc = bacc.Bacc("TRN2", target_bir_lowering=False, num_devices=1)
    xT_dram = nc.dram_tensor("xT", xT.shape, F32, kind="ExternalInput").ap()
    ctxT_dram = nc.dram_tensor("ctxT", ctxT.shape, F32, kind="ExternalInput").ap()
    outT_dram = nc.dram_tensor("outT", xT.shape, F32, kind="ExternalOutput").ap()
    cross_attention(nc, xT_dram, ctxT_dram, outT_dram)
    result = run_bass_kernel_spmd(nc, [{"xT": xT, "ctxT": ctxT}], core_ids=[0])
    outT = result.results[0]["outT"]
    return np.ascontiguousarray(outT.transpose(0, 2, 4, 3, 1)).reshape(B, R, D)
```
